# Optimizing a Trainium2 kernel written in Bass

```python
import numpy as np
import jax
import jax.numpy as jnp

def _softmax(x, axis=-1):
    return jax.nn.softmax(x, axis=axis)

def _gelu(x):
    return jax.nn.gelu(x, approximate=True)

def _silu(x):
    return jax.nn.silu(x)

def _sigmoid(x):
    return jax.nn.sigmoid(x)

def _layernorm(x, axis=-1, eps=1e-05):
    m = jnp.mean(x, axis=axis, keepdims=True)
    v = jnp.var(x, axis=axis, keepdims=True)
    return (x - m) / jnp.sqrt(v + eps)

def _scatter_add(tgt, idx, src, axis=0):
    return tgt.at[idx].add(src)

def _segment_sum(src, seg, n):
    return jax.ops.segment_sum(src, seg, n)
kernel_name = 'mk_rec_standalone_d1_rec_r8_b7d4d0'

def setup_inputs(seed: int=0):
    np.random.seed(seed)
    _w = jnp.asarray

    def _rec_inputs():
        import jax
        import jax.numpy as jnp
        _rk = jax.random.key(seed)
        r_onehot_i = jnp.stack([jax.random.randint(jax.random.fold_in(jax.random.fold_in(_rk, 1), 0), (1024,), 17, 99983, jnp.int32), jax.random.randint(jax.random.fold_in(jax.random.fold_in(_rk, 1), 1), (1024,), 22, 99987, jnp.int32), jax.random.randint(jax.random.fold_in(jax.random.fold_in(_rk, 1), 2), (1024,), 7, 99990, jnp.int32), jax.random.randint(jax.random.fold_in(jax.random.fold_in(_rk, 1), 3), (1024,), 6, 99987, jnp.int32), jax.random.randint(jax.random.fold_in(jax.random.fold_in(_rk, 1), 4), (1024,), 5, 99993, jnp.int32), jax.random.randint(jax.random.fold_in(jax.random.fold_in(_rk, 1), 5), (1024,), 14, 99970, jnp.int32), jax.random.randint(jax.random.fold_in(jax.random.fold_in(_rk, 1), 6), (1024,), 6, 99988, jnp.int32), jax.random.randint(jax.random.fold_in(jax.random.fold_in(_rk, 1), 7), (1024,), 10, 99987, jnp.int32), jax.random.randint(jax.random.fold_in(jax.random.fold_in(_rk, 1), 8), (1024,), 3, 99998, jnp.int32), jax.random.randint(jax.random.fold_in(jax.random.fold_in(_rk, 1), 9), (1024,), 13, 99991, jnp.int32), jax.random.randint(jax.random.fold_in(jax.random.fold_in(_rk, 1), 10), (1024,), 39, 99987, jnp.int32), jax.random.randint(jax.random.fold_in(jax.random.fold_in(_rk, 1), 11), (1024,), 1, 99994, jnp.int32), jax.random.randint(jax.random.fold_in(jax.random.fold_in(_rk, 1), 12), (1024,), 22, 99998, jnp.int32), jax.random.randint(jax.random.fold_in(jax.random.fold_in(_rk, 1), 13), (1024,), 11, 99980, jnp.int32), jax.random.randint(jax.random.fold_in(jax.random.fold_in(_rk, 1), 14), (1024,), 5, 99967, jnp.int32), jax.random.randint(jax.random.fold_in(jax.random.fold_in(_rk, 1), 15), (1024,), 2, 99998, jnp.int32), jax.random.randint(jax.random.fold_in(jax.random.fold_in(_rk, 1), 16), (1024,), 1, 99995, jnp.int32), jax.random.randint(jax.random.fold_in(jax.random.fold_in(_rk, 1), 17), (1024,), 4, 99996, jnp.int32), jax.random.randint(jax.random.fold_in(jax.random.fold_in(_rk, 1), 18), (1024,), 7, 99996, jnp.int32), jax.random.randint(jax.random.fold_in(jax.random.fold_in(_rk, 1), 19), (1024,), 4, 99990, jnp.int32)], axis=1)
        r_mh_i = jax.random.randint(jax.random.fold_in(_rk, 2), (2, 1024, 50), 0, 12500, jnp.int32)
        return (r_onehot_i, r_mh_i)
    r_onehot_i, r_mh_i = _rec_inputs()

    def _L0_rec_setup():
        import jax, jax.numpy as jnp
        import numpy as np
        NUM_EMB = 12500
        EMB = 64
        NUM_CTNS = 10
        HEADS = 4
        ATT = 32
        HD = HEADS * ATT
        FIELDS = 32
        B = 1024

        def _linear_params(key, out_f, in_f):
            kw, kb = jax.random.split(key)
            W = jax.random.normal(kw, (out_f, in_f), jnp.float32) * 0.05
            b = jax.random.normal(kb, (out_f,), jnp.float32) * 0.05
            return (W, b)

        def _attn_block(y, QW, Qb, KW, Kb, VW, Vb, RW, Rb):
            b, f, _ = y.shape
            Q = (y @ QW.T + Qb).reshape(b, f, HEADS, ATT)
            K = (y @ KW.T + Kb).reshape(b, f, HEADS, ATT)
            V = (y @ VW.T + Vb).reshape(b, f, HEADS, ATT)
            Res = y @ RW.T + Rb
            scores = jnp.einsum('bqhd,bkhd->bhqk', Q, K)
            A = jax.nn.softmax(scores, axis=-1)
            O = jnp.einsum('bhqk,bkhd->bqhd', A, V).reshape(b, f, HD)
            return jax.nn.relu(O + Res)
        key = jax.random.key(seed)
        ks = jax.random.split(key, 16)
        inp = {'onehot_i': jax.random.randint(ks[0], (B, 20), 0, NUM_EMB), 'onehot_x': jax.random.uniform(ks[1], (B, 20), jnp.float32), 'mh_i': jax.random.randint(ks[2], (2, B, 50), 0, NUM_EMB), 'mh_x': jax.random.uniform(ks[3], (2, B, 50), jnp.float32), 'ctns': jax.random.normal(ks[4], (B, NUM_CTNS), jnp.float32), 'xx': jax.random.normal(ks[5], (NUM_EMB, EMB), jnp.float32), 'xy': jax.random.normal(ks[6], (NUM_CTNS, EMB), jnp.float32)}
        names1 = ['QW1', 'Qb1', 'KW1', 'Kb1', 'VW1', 'Vb1', 'RW1', 'Rb1']
        for i in range(4):
            W, b = _linear_params(ks[7 + i], HD, EMB)
            inp[names1[2 * i]] = W
            inp[names1[2 * i + 1]] = b
        names2 = ['QW2', 'Qb2', 'KW2', 'Kb2', 'VW2', 'Vb2', 'RW2', 'Rb2']
        for i in range(4):
            W, b = _linear_params(ks[11 + i], HD, HD)
            inp[names2[2 * i]] = W
            inp[names2[2 * i + 1]] = b
        lW, lb = _linear_params(ks[15], 1, FIELDS * HD)
        inp['logitW'] = lW
        inp['logitb'] = lb
        return inp
    _L0_rec_all = _L0_rec_setup()
    _L0_rec_in = {k: v for k, v in _L0_rec_all.items() if k in ('onehot_x', 'mh_x', 'ctns', 'xx', 'xy', 'QW1', 'Qb1', 'KW1', 'Kb1', 'VW1', 'Vb1', 'RW1', 'Rb1', 'QW2', 'Qb2', 'KW2', 'Kb2', 'VW2', 'Vb2', 'RW2', 'Rb2', 'logitW', 'logitb')}
    del _L0_rec_all
    return {'r_onehot_i': r_onehot_i, 'r_mh_i': r_mh_i, 'L0_rec_onehot_x': _L0_rec_in['onehot_x'], 'L0_rec_mh_x': _L0_rec_in['mh_x'], 'L0_rec_ctns': _L0_rec_in['ctns'], 'L0_rec_xx': _L0_rec_in['xx'], 'L0_rec_xy': _L0_rec_in['xy'], 'L0_rec_QW1': _L0_rec_in['QW1'], 'L0_rec_Qb1': _L0_rec_in['Qb1'], 'L0_rec_KW1': _L0_rec_in['KW1'], 'L0_rec_Kb1': _L0_rec_in['Kb1'], 'L0_rec_VW1': _L0_rec_in['VW1'], 'L0_rec_Vb1': _L0_rec_in['Vb1'], 'L0_rec_RW1': _L0_rec_in['RW1'], 'L0_rec_Rb1': _L0_rec_in['Rb1'], 'L0_rec_QW2': _L0_rec_in['QW2'], 'L0_rec_Qb2': _L0_rec_in['Qb2'], 'L0_rec_KW2': _L0_rec_in['KW2'], 'L0_rec_Kb2': _L0_rec_in['Kb2'], 'L0_rec_VW2': _L0_rec_in['VW2'], 'L0_rec_Vb2': _L0_rec_in['Vb2'], 'L0_rec_RW2': _L0_rec_in['RW2'], 'L0_rec_Rb2': _L0_rec_in['Rb2'], 'L0_rec_logitW': _L0_rec_in['logitW'], 'L0_rec_logitb': _L0_rec_in['logitb']}

def reference(r_onehot_i, r_mh_i, L0_rec_onehot_x, L0_rec_mh_x, L0_rec_ctns, L0_rec_xx, L0_rec_xy, L0_rec_QW1, L0_rec_Qb1, L0_rec_KW1, L0_rec_Kb1, L0_rec_VW1, L0_rec_Vb1, L0_rec_RW1, L0_rec_Rb1, L0_rec_QW2, L0_rec_Qb2, L0_rec_KW2, L0_rec_Kb2, L0_rec_VW2, L0_rec_Vb2, L0_rec_RW2, L0_rec_Rb2, L0_rec_logitW, L0_rec_logitb):
    import jax
    import jax.numpy as jnp

    def _L0_rec_ref(onehot_i, onehot_x, mh_i, mh_x, ctns, xx, xy, QW1, Qb1, KW1, Kb1, VW1, Vb1, RW1, Rb1, QW2, Qb2, KW2, Kb2, VW2, Vb2, RW2, Rb2, logitW, logitb):
        import jax, jax.numpy as jnp
        import numpy as np
        NUM_EMB = 12500
        EMB = 64
        NUM_CTNS = 10
        HEADS = 4
        ATT = 32
        HD = HEADS * ATT
        FIELDS = 32
        B = 1024

        def _linear_params(key, out_f, in_f):
            kw, kb = jax.random.split(key)
            W = jax.random.normal(kw, (out_f, in_f), jnp.float32) * 0.05
            b = jax.random.normal(kb, (out_f,), jnp.float32) * 0.05
            return (W, b)

        def _attn_block(y, QW, Qb, KW, Kb, VW, Vb, RW, Rb):
            b, f, _ = y.shape
            Q = (y @ QW.T + Qb).reshape(b, f, HEADS, ATT)
            K = (y @ KW.T + Kb).reshape(b, f, HEADS, ATT)
            V = (y @ VW.T + Vb).reshape(b, f, HEADS, ATT)
            Res = y @ RW.T + Rb
            scores = jnp.einsum('bqhd,bkhd->bhqk', Q, K)
            A = jax.nn.softmax(scores, axis=-1)
            O = jnp.einsum('bhqk,bkhd->bqhd', A, V).reshape(b, f, HD)
            return jax.nn.relu(O + Res)
        onehot_fields = xx[onehot_i] * onehot_x[..., None]
        mh_fields = (xx[mh_i] * mh_x[..., None]).sum(axis=2)
        mh_fields = jnp.transpose(mh_fields, (1, 0, 2))
        ctns_fields = ctns[..., None] * xy
        y = jnp.concatenate([onehot_fields, mh_fields, ctns_fields], axis=1)
        y = _attn_block(y, QW1, Qb1, KW1, Kb1, VW1, Vb1, RW1, Rb1)
        y = _attn_block(y, QW2, Qb2, KW2, Kb2, VW2, Vb2, RW2, Rb2)
        flat = y.reshape(y.shape[0], -1)
        out = jax.nn.sigmoid(flat @ logitW.T + logitb)
        return out.squeeze()
    y = _L0_rec_ref(r_onehot_i, L0_rec_onehot_x, r_mh_i, L0_rec_mh_x, L0_rec_ctns, L0_rec_xx, L0_rec_xy, L0_rec_QW1, L0_rec_Qb1, L0_rec_KW1, L0_rec_Kb1, L0_rec_VW1, L0_rec_Vb1, L0_rec_RW1, L0_rec_Rb1, L0_rec_QW2, L0_rec_Qb2, L0_rec_KW2, L0_rec_Kb2, L0_rec_VW2, L0_rec_Vb2, L0_rec_RW2, L0_rec_Rb2, L0_rec_logitW, L0_rec_logitb)
    return y

_drawn_inputs = setup_inputs


def setup_inputs(seed=0):
    import zlib

    import numpy as np

    out = dict(_drawn_inputs(seed))
    spreads = {}
    factors = {}
    for name, (base, spread) in spreads.items():
        noise = np.random.default_rng([zlib.crc32(name.encode()), seed]).standard_normal(out[name].shape)
        drawn = base * np.exp(spread * noise) if base else spread * noise
        out[name] = jnp.asarray(drawn.astype(out[name].dtype))
    for name, factor in factors.items():
        out[name] = (out[name] * factor).astype(out[name].dtype)
    return out
```

```python
from contextlib import ExitStack

import concourse.bass as bass
from concourse import mybir

F32 = mybir.dt.float32
I32 = mybir.dt.int32
U32 = mybir.dt.uint32
ALU = mybir.AluOpType
ACT = mybir.ActivationFunctionType
AX = mybir.AxisListType

P = 128
SAMPLES = 1024
FIELDS = 32
ONEHOT = 20
MULTI = 2
CONT = 10
BAG = 50
ROWS = 12500
EMB = 64
HD = 128
HEADS = 4
ATT = 32
UNIT = 16
UNITS = SAMPLES // UNIT
BLOCK = 2 * UNIT
BLOCKS = SAMPLES // BLOCK
QUARTERS = 4
OH_SLOTS = ONEHOT // QUARTERS
MH_SLOTS = MULTI * BAG // QUARTERS
SLOTS = OH_SLOTS + MH_SLOTS
CHUNK = SLOTS // 2
MH_FIRST = CHUNK - OH_SLOTS
COLS = UNIT * FIELDS
DMA = 16
LOOP_FIRST = 3
LOOP_UNITS = 4
LOOP_TRIPS = 13


class Unit:

    def __init__(self, base, offset, quarter=None):
        self.base, self.offset, self.quarter_base = base, offset, quarter

    def __add__(self, k):
        return Unit(self.base, self.offset + k, self.quarter_base)

    def number(self):
        return self.offset if self.base is None else self.base + self.offset

    def quarter(self):
        n = self.offset // 4
        return n if self.base is None else self.quarter_base + n

    def mod(self, k):
        return self.offset % k

    def inside(self, first, last):
        return self.base is not None or first <= self.offset <= last


def wait(engine, semaphore, unit, k):
    if unit.base is not None:
        engine.wait_ge(semaphore, unit.base + (unit.offset + k))
    elif unit.offset + k > 0:
        engine.wait_ge(semaphore, unit.offset + k)


def run_units(engine, first, last, one):
    loop_end = LOOP_FIRST + LOOP_UNITS * LOOP_TRIPS
    for n in range(first, LOOP_FIRST):
        one(Unit(None, n))
    with engine.Fori(0, LOOP_TRIPS) as trip:
        base = engine.snap(trip * LOOP_UNITS)
        for r in range(LOOP_UNITS):
            one(Unit(base, LOOP_FIRST + r, trip))
    for n in range(loop_end, last + 1):
        one(Unit(None, n))


def build(nc, a, out):
    with ExitStack() as ctx:
        def sb(name, shape, dt=F32):
            return ctx.enter_context(nc.sbuf_tensor(name, shape, dt))

        def psum(name, shape):
            return ctx.enter_context(nc.psum_tensor(name, shape, F32))

        def sem(name):
            return ctx.enter_context(nc.semaphore(name))

        idx_raw = sb("idx_raw", [P, BLOCKS * SLOTS], I32)
        idx_wrap = sb("idx_wrap", [P, BLOCKS * SLOTS], I32)
        idx_all = sb("idx_all", [P, BLOCKS * SLOTS], I32)
        x_all = sb("x_all", [P, BLOCKS * SLOTS])
        ctns_t = sb("ctns_t", [CONT, SAMPLES])
        xy_wide = sb("xy_wide", [CONT, P])
        ident = sb("ident", [P, P])
        w1 = sb("w1", [EMB, 4, HD])
        w2 = sb("w2", [P, 4, HD])
        bias = sb("bias", [P, 8])
        out_bias = sb("out_bias", [P, 2])
        logit_w = sb("logit_w", [P, FIELDS])
        logit_b = sb("logit_b", [P, 1])
        neg_logit_b = sb("neg_logit_b", [P, 1])
        ones = sb("ones", [P, 1])
        ctns_diag = sb("ctns_diag", [CONT, SAMPLES * CONT])
        bag_sum = sb("bag_sum", [P, MULTI * BLOCK])

        idx_now = [sb(f"idx_now{b}", [P, SLOTS], I32) for b in range(2)]
        rows = [sb(f"rows{b}", [P, SLOTS, EMB]) for b in range(2)]
        scaled = [sb(f"scaled{b}", [P, OH_SLOTS, EMB]) for b in range(2)]
        bag_part = [sb(f"bag_part{c}", [P, EMB]) for c in range(2)]
        bag = [sb(f"bag{b}", [P, EMB]) for b in range(2)]

        y1 = [sb(f"y1_{b}", [EMB, COLS]) for b in range(2)]
        y2 = [sb(f"y2_{b}", [P, COLS]) for b in range(2)]
        qt = [sb(f"qt{n}", [P, COLS]) for n in range(2)]
        kt = [sb(f"kt{n}", [P, COLS]) for n in range(2)]
        v1 = [sb(f"v1_{b}", [P, COLS]) for b in range(2)]
        v2 = sb("v2", [P, COLS])
        row_max = [sb(f"row_max{n}", [P, UNIT]) for n in range(2)]
        row_sum = [sb(f"row_sum{n}", [P, UNIT]) for n in range(2)]
        row_inv = [sb(f"row_inv{n}", [P, UNIT]) for n in range(2)]
        shifted = [sb(f"shifted{n}", [P, COLS]) for n in range(2)]
        probs = [sb(f"probs{n}", [P, COLS]) for n in range(2)]
        normed = [sb(f"normed{n}", [P, COLS]) for n in range(2)]
        at = [sb(f"at{n}", [P, COLS]) for n in range(2)]
        z = sb("z", [P, COLS])
        weighted = sb("weighted", [P, COLS])
        logit_part = sb("logit_part", [P, SAMPLES])
        expd = sb("expd", [P, SAMPLES // P])
        denom = sb("denom", [P, SAMPLES // P])
        answer = sb("answer", [P, SAMPLES // P])

        ps_y = psum("ps_y", [P, COLS])
        ps_q = psum("ps_q", [P, COLS])
        ps_k = psum("ps_k", [P, COLS])
        ps_v = psum("ps_v", [P, COLS])
        ps_s = [psum(f"ps_s{n}", [P, COLS]) for n in range(2)]
        ps_o = [psum(f"ps_o{n}", [P, COLS]) for n in range(2)]

        idx_loaded = sem("idx_loaded")
        x_loaded = sem("x_loaded")
        const_loaded = sem("const_loaded")
        layer_loaded = sem("layer_loaded")
        idx_step = sem("idx_step")
        idx_ready = sem("idx_ready")
        gathered = [[sem(f"gathered{b}{c}") for c in range(2)] for b in range(2)]
        consts_ready = sem("consts_ready")
        onehot_scaled = sem("onehot_scaled")
        bag_scaled = sem("bag_scaled")
        chunk_done = sem("chunk_done")
        bag_ready = sem("bag_ready")
        y_out = sem("y_out")
        y1_ready = sem("y1_ready")
        qkv_out = [sem(f"qkv_out{n}") for n in range(2)]
        q_ready = [sem(f"q_ready{n}") for n in range(2)]
        k_ready = [sem(f"k_ready{n}") for n in range(2)]
        v_ready = [sem(f"v_ready{n}") for n in range(2)]
        scores_out = [sem(f"scores_out{n}") for n in range(2)]
        max_done = [sem(f"max_done{n}") for n in range(2)]
        shift_done = [sem(f"shift_done{n}") for n in range(2)]
        exp_done = [sem(f"exp_done{n}") for n in range(2)]
        sum_done = [sem(f"sum_done{n}") for n in range(2)]
        inv_done = [sem(f"inv_done{n}") for n in range(2)]
        norm_done = [sem(f"norm_done{n}") for n in range(2)]
        at_ready = [sem(f"at_ready{n}") for n in range(2)]
        o_out = [sem(f"o_out{n}") for n in range(2)]
        relu_done = [sem(f"relu_done{n}") for n in range(2)]
        weighted_done = sem("weighted_done")
        logit_done = sem("logit_done")
        logits_out = sem("logits_out")
        exp_out = sem("exp_out")
        denom_ready = sem("denom_ready")
        answer_ready = sem("answer_ready")
        stored = sem("stored")
        pe_gate = sem("pe_gate")
        pool_gate = sem("pool_gate")

        def by_key(t):
            return t[:, :].rearrange("p (s k) -> p s k", k=FIELDS)

        def over_keys(t):
            return t[:, :].unsqueeze(2).to_broadcast([P, UNIT, FIELDS])

        block = ctx.enter_context(nc.Block())

        @block.sync
        def _(sp):
            sp.dma_start(idx_raw[:, :], a["idx"]).then_inc(idx_loaded, DMA)
            sp.dma_start(x_all[:, :], a["x"]).then_inc(x_loaded, DMA)
            sp.dma_start(w1[:, :, :], a["w1"]).then_inc(layer_loaded, DMA)
            sp.dma_start(w2[:, :, :], a["w2"]).then_inc(layer_loaded, DMA)
            sp.dma_start(logit_w[:, :], a["logit_w"]).then_inc(layer_loaded, DMA)
            sp.wait_ge(answer_ready, 1)
            sp.dma_start(out.rearrange("(p n) -> p n", p=P), answer[:, :]).then_inc(stored, DMA)
            sp.wait_ge(stored, DMA)

        @block.gpsimd
        def _(pool):
            def gather_block(parity, n, free):
                for c in range(2):
                    if c == 0:
                        pool.wait_ge(idx_ready, n + 1)
                    if free is not None:
                        pool.wait_ge(chunk_done, free + c)
                    pool.sem_inc(pool_gate, 1)
                    for t in range(c * CHUNK, (c + 1) * CHUNK):
                        pool.indirect_dma_start(
                            rows[parity][:, t, :], None, a["xx"],
                            bass.IndirectOffsetOnAxis(ap=idx_now[parity][:, t:t + 1].bitcast(U32), axis=0),
                        ).then_inc(gathered[parity][c], DMA)

            gather_block(0, 0, None)
            gather_block(1, 1, None)
            with pool.Fori(1, BLOCKS // 2) as pair:
                two = pool.snap(pair * 2)
                four = pool.snap(pair * 4)
                gather_block(0, two, four - 3)
                gather_block(1, two + 1, four - 1)

        @block.tensor
        def _(pe):
            def fields_in(u):
                half = UNIT * u.mod(2)
                parity = u.mod(4) // 2
                pe.wait_ge(bag_ready, (u.quarter() * 2 + parity) + 1)
                wait(pe, y1_ready, u, 0)
                y = ps_y[:, :].rearrange("p (s f) -> p s f", f=FIELDS)
                first = u.number() * (UNIT * CONT)
                nc.tensor.matmul(y[:, :, ONEHOT + MULTI:],
                                 xy_wide[:, :], ctns_diag[:, bass.ds(first, UNIT * CONT)].rearrange("p (s c) -> p s c", c=CONT),
                                 start=True, stop=True)
                picks = ident[:, :].rearrange("p (q s) -> p q s", s=BLOCK)[:, :, half:half + UNIT]
                for t in range(OH_SLOTS):
                    fields = y[0:EMB, :, t:ONEHOT:OH_SLOTS].rearrange("p s q -> p q s")
                    nc.tensor.matmul(fields, scaled[parity][:, t, :], picks, start=True, stop=True)
                sums = bag_sum[:, :].rearrange("p (f s) -> p f s", f=MULTI)[:, :, half:half + UNIT]
                nc.tensor.matmul(y[0:EMB, :, ONEHOT:ONEHOT + MULTI].rearrange("p s f -> p f s"),
                                 bag[parity][:, :], sums, start=True, stop=True).then_inc(y_out, 1)

            def projections(n, u, y, w):
                for j, ps in enumerate((ps_q, ps_k, ps_v)):
                    last = nc.tensor.matmul(ps[:, :], w[:, j, :], y[:, :], start=True, stop=True)
                    last.then_inc(qkv_out[n], 1)

            def scores(n, u):
                for s in range(UNIT):
                    c = slice(s * FIELDS, (s + 1) * FIELDS)
                    for h in range(HEADS):
                        r = slice(h * ATT, (h + 1) * ATT)
                        last = nc.tensor.matmul(ps_s[n][r, c], qt[n][r, c], kt[n][r, c], start=True, stop=True,
                                                tile_position=(h * ATT, h * ATT))
                last.then_inc(scores_out[n], 1)

            def output(n, u, y, w, v):
                nc.tensor.matmul(ps_o[n][:, :], w[:, 3, :], y[:, :], start=True, stop=False)
                wait(pe, at_ready[n], u, 1)
                pe.sem_inc(pe_gate, 1)
                for s in range(UNIT):
                    c = slice(s * FIELDS, (s + 1) * FIELDS)
                    for h in range(HEADS):
                        r = slice(h * ATT, (h + 1) * ATT)
                        last = nc.tensor.matmul(ps_o[n][r, c], v[r, c], at[n][r, c], start=False, stop=s == UNIT - 1,
                                                tile_position=(h * ATT, h * ATT))
                last.then_inc(o_out[n], 1)

            def step(i):
                if i.inside(0, UNITS - 1):
                    wait(pe, q_ready[0], i, 1)
                    wait(pe, k_ready[0], i, 1)
                    wait(pe, shift_done[0], i, 0)
                    pe.sem_inc(pe_gate, 1)
                    scores(0, i)
                if i.inside(-1, UNITS - 2):
                    fields_in(i + 1)
                if i.inside(2, UNITS + 1):
                    u = i + -2
                    wait(pe, relu_done[1], u, 0)
                    output(1, u, y2[u.mod(2)], w2, v2)
                if i.inside(1, UNITS):
                    u = i + -1
                    wait(pe, relu_done[0], u, 1)
                    if i.inside(1, UNITS - 1):
                        wait(pe, v_ready[0], i, 1)
                    else:
                        wait(pe, v_ready[1], u, 0)
                    projections(1, u, y2[u.mod(2)], w2)
                if i.inside(-1, UNITS - 2):
                    u = i + 1
                    wait(pe, y1_ready, u, 1)
                    wait(pe, q_ready[1], i, 0)
                    wait(pe, k_ready[1], i, 0)
                    if i.inside(1, UNITS - 2):
                        wait(pe, v_ready[1], i, 0)
                    else:
                        wait(pe, v_ready[0], i, 1)
                    projections(0, u, y1[u.mod(2)], w1)
                if i.inside(1, UNITS):
                    u = i + -1
                    wait(pe, q_ready[1], u, 1)
                    wait(pe, k_ready[1], u, 1)
                    wait(pe, shift_done[1], u, 0)
                    pe.sem_inc(pe_gate, 1)
                    scores(1, u)
                if i.inside(0, UNITS - 1):
                    wait(pe, relu_done[0], i, 0)
                    output(0, i, y1[i.mod(2)], w1, v1[i.mod(2)])

            pe.wait_ge(layer_loaded, 3 * DMA)
            pe.wait_ge(const_loaded, 5 * DMA)
            pe.wait_ge(consts_ready, 5)
            run_units(pe, -1, UNITS + 1, step)

            pe.wait_ge(logit_done, UNITS)
            per = SAMPLES // P
            part = logit_part[:, :].rearrange("c (p n) -> c n p", n=per)
            for n in range(per):
                last = nc.tensor.matmul(ps_y[:, n:n + 1], part[:, n, :], ones[:, :], start=True, stop=True)
            last.then_inc(logits_out, 1)

        @block.scalar
        def _(act):
            act.dma_start(ident[:, :], a["ident"]).then_inc(const_loaded, DMA)
            act.dma_start(ctns_t[:, :], a["ctns_t"]).then_inc(const_loaded, DMA)
            act.dma_start(xy_wide[:, 0:EMB], a["xy"]).then_inc(const_loaded, DMA)
            act.dma_start(bias[:, :], a["bias"]).then_inc(const_loaded, DMA)
            act.dma_start(logit_b[:, :], a["logit_b"]).then_inc(const_loaded, DMA)

            def evacuate(n, u):
                act.wait_ge(qkv_out[n], u.number() * 3 + 1)
                nc.scalar.activation(qt[n][:, :], ps_q[:, :], ACT.Identity,
                                     bias=bias[:, 4 * n:4 * n + 1]).then_inc(q_ready[n], 1)
                act.wait_ge(qkv_out[n], u.number() * 3 + 2)
                nc.scalar.activation(kt[n][:, :], ps_k[:, :], ACT.Identity,
                                     bias=bias[:, 4 * n + 1:4 * n + 2]).then_inc(k_ready[n], 1)

            def exponential(n, u):
                wait(act, shift_done[n], u, 1)
                wait(act, norm_done[n], u, 0)
                nc.scalar.activation(probs[n][:, :], shifted[n][:, :], ACT.Exp).then_inc(exp_done[n], 1)

            def relu(n, u, y):
                wait(act, o_out[n], u, 1)
                nc.scalar.activation(y[:, :], ps_o[n][:, :], ACT.Relu,
                                     bias=out_bias[:, n:n + 1]).then_inc(relu_done[n], 1)

            def step(i):
                if i.inside(-1, UNITS - 2):
                    u = i + 1
                    wait(act, y_out, u, 1)
                    wait(act, o_out[0], i, 0)
                    nc.scalar.activation(y1[u.mod(2)][:, :], ps_y[0:EMB, :], ACT.Copy).then_inc(y1_ready, 1)
                if i.inside(0, UNITS - 1):
                    exponential(0, i)
                if i.inside(2, UNITS + 1):
                    wait(act, weighted_done, i, -2)
                    relu(1, i + -2, z)
                if i.inside(1, UNITS):
                    evacuate(1, i + -1)
                if i.inside(-1, UNITS - 2):
                    evacuate(0, i + 1)
                if i.inside(1, UNITS):
                    exponential(1, i + -1)
                if i.inside(0, UNITS - 1):
                    wait(act, o_out[1], i, -1)
                    relu(0, i, y2[i.mod(2)])

            act.wait_ge(const_loaded, 5 * DMA)
            act.wait_ge(consts_ready, 5)
            run_units(act, -1, UNITS + 1, step)

            act.wait_ge(logits_out, 1)
            nc.scalar.activation(expd[:, :], ps_y[:, 0:SAMPLES // P], ACT.Exp, scale=-1.0,
                                 bias=neg_logit_b[:, :]).then_inc(exp_out, 1)

        @block.vector
        def _(dve):
            def wrap_indices(lo, hi, count):
                c = slice(lo * SLOTS, hi * SLOTS)
                nc.vector.tensor_scalar(idx_wrap[:, c], idx_raw[:, c], 0.0, float(ROWS),
                                        ALU.is_lt, ALU.mult).then_inc(idx_step, 1)
                dve.wait_ge(idx_step, count + 1)
                nc.vector.tensor_tensor(idx_wrap[:, c], idx_raw[:, c], idx_wrap[:, c], ALU.add).then_inc(idx_step, 1)
                dve.wait_ge(idx_step, count + 2)
                nc.vector.tensor_scalar(idx_all[:, c], idx_wrap[:, c], 0.0, float(ROWS - 1),
                                        ALU.max, ALU.min).then_inc(idx_step, 1)
                dve.wait_ge(idx_step, count + 3)

            def chunk(m):
                c = m.mod(2)
                parity = m.mod(4) // 2
                half_block = m.quarter()
                dve.wait_ge(gathered[parity][c], (half_block + 1) * (DMA * CHUNK))
                first = (half_block * 2 + parity) * SLOTS
                t0, t1 = (OH_SLOTS, CHUNK) if c == 0 else (CHUNK, SLOTS)
                if c == 0:
                    wait(dve, y_out, m, -2)
                    nc.vector.tensor_tensor(
                        scaled[parity][:, :, :], rows[parity][:, 0:OH_SLOTS, :],
                        x_all[:, bass.ds(first, OH_SLOTS)].unsqueeze(2).to_broadcast([P, OH_SLOTS, EMB]),
                        ALU.mult).then_inc(onehot_scaled, 1)
                bag_rows = rows[parity][:, t0:t1, :]
                nc.vector.tensor_tensor(
                    bag_rows, bag_rows,
                    x_all[:, bass.ds(first + t0, t1 - t0)].unsqueeze(2).to_broadcast([P, t1 - t0, EMB]),
                    ALU.mult).then_inc(bag_scaled, 1)
                wait(dve, bag_scaled, m, 1)
                nc.vector.tensor_reduce(bag_part[c][:, :], bag_rows.rearrange("p t e -> p e t"), AX.X,
                                        ALU.add).then_inc(chunk_done, 1)
                if c == 1:
                    wait(dve, chunk_done, m, 1)
                    nc.vector.tensor_tensor(bag[parity][:, :], bag_part[0][:, :], bag_part[1][:, :],
                                            ALU.add).then_inc(bag_ready, 1)
                    if m.inside(0, UNITS - 5):
                        nc.vector.tensor_copy(
                            idx_now[parity][:, :],
                            idx_all[:, bass.ds(first + 2 * SLOTS, SLOTS)]).then_inc(idx_ready, 1)

            def values(n, u, v):
                dve.wait_ge(qkv_out[n], u.number() * 3 + 3)
                nc.vector.transpose(v[:, :], ps_v[:, :]).then_inc(v_ready[n], 1)

            def shift(n, u):
                wait(dve, scores_out[n], u, 1)
                nc.vector.tensor_reduce(row_max[n][:, :], by_key(ps_s[n]), AX.X, ALU.max).then_inc(max_done[n], 1)
                wait(dve, max_done[n], u, 1)
                wait(dve, exp_done[n], u, 0)
                nc.vector.tensor_tensor(by_key(shifted[n]), by_key(ps_s[n]), over_keys(row_max[n]),
                                        ALU.subtract).then_inc(shift_done[n], 1)

            def normalise(n, u):
                wait(dve, exp_done[n], u, 1)
                nc.vector.tensor_reduce(row_sum[n][:, :], by_key(probs[n]), AX.X, ALU.add).then_inc(sum_done[n], 1)
                wait(dve, sum_done[n], u, 1)
                nc.vector.reciprocal(row_inv[n][:, :], row_sum[n][:, :]).then_inc(inv_done[n], 1)
                wait(dve, inv_done[n], u, 1)
                nc.vector.tensor_tensor(by_key(normed[n]), by_key(probs[n]), over_keys(row_inv[n]),
                                        ALU.mult).then_inc(norm_done[n], 1)
                wait(dve, norm_done[n], u, 1)
                wait(dve, o_out[n], u, 0)
                nc.vector.transpose(at[n][:, :], normed[n][:, :]).then_inc(at_ready[n], 1)

            def logit(u):
                wait(dve, relu_done[1], u, 1)
                nc.vector.tensor_tensor(
                    by_key(weighted), by_key(z), logit_w[:, :].unsqueeze(1).to_broadcast([P, UNIT, FIELDS]),
                    ALU.mult).then_inc(weighted_done, 1)
                wait(dve, weighted_done, u, 1)
                nc.vector.tensor_reduce(logit_part[:, bass.ds(u.number() * UNIT, UNIT)], by_key(weighted), AX.X,
                                        ALU.add).then_inc(logit_done, 1)

            def step(i):
                if i.inside(0, UNITS - 1):
                    shift(0, i)
                if i.inside(-1, UNITS - 4):
                    chunk(i + 3)
                if i.inside(0, UNITS - 1):
                    normalise(0, i)
                if i.inside(2, UNITS + 1):
                    logit(i + -2)
                if i.inside(1, UNITS):
                    values(1, i + -1, v2)
                if i.inside(-1, UNITS - 2):
                    values(0, i + 1, v1[(i + 1).mod(2)])
                if i.inside(1, UNITS):
                    shift(1, i + -1)
                    normalise(1, i + -1)

            dve.wait_ge(idx_loaded, DMA)
            wrap_indices(0, 2, 0)
            for b in range(2):
                nc.vector.tensor_copy(idx_now[b][:, :], idx_all[:, b * SLOTS:(b + 1) * SLOTS]).then_inc(idx_ready, 1)
            wrap_indices(2, BLOCKS, 3)
            nc.vector.memset(xy_wide[:, EMB:P], 0.0).then_inc(consts_ready, 1)
            nc.vector.memset(ones[:, :], 1.0).then_inc(consts_ready, 1)
            dve.wait_ge(const_loaded, 5 * DMA)
            nc.vector.tensor_tensor(out_bias[:, :], bias[:, 2::4], bias[:, 3::4], ALU.add).then_inc(consts_ready, 1)
            nc.vector.tensor_tensor(
                ctns_diag[:, :].rearrange("p (s c) -> p s c", c=CONT),
                ctns_t[:, :].unsqueeze(2).to_broadcast([CONT, SAMPLES, CONT]),
                ident[0:CONT, 0:CONT].unsqueeze(1).to_broadcast([CONT, SAMPLES, CONT]),
                ALU.mult).then_inc(consts_ready, 1)
            halves = ident[:, :].rearrange("p (f h s) -> p h f s", f=MULTI, h=2)
            nc.vector.tensor_tensor(bag_sum[:, :].rearrange("p (f s) -> p f s", f=MULTI),
                                    halves[:, 0], halves[:, 1], ALU.add).then_inc(consts_ready, 1)
            nc.vector.tensor_scalar(neg_logit_b[:, :], logit_b[:, :], -1.0, None, ALU.mult).then_inc(consts_ready, 1)
            dve.wait_ge(layer_loaded, 3 * DMA)
            dve.wait_ge(x_loaded, DMA)
            chunk(Unit(None, 0))
            chunk(Unit(None, 1))
            run_units(dve, -1, UNITS + 1, step)

            dve.wait_ge(exp_out, 1)
            nc.vector.tensor_scalar(denom[:, :], expd[:, :], 1.0, None, ALU.add).then_inc(denom_ready, 1)
            dve.wait_ge(denom_ready, 1)
            nc.vector.reciprocal(answer[:, :], denom[:, :]).then_inc(answer_ready, 1)


def kernel(**inputs):
    import numpy as np
    import concourse.bacc as bacc
    from concourse.bass_utils import run_bass_kernel_spmd

    def get(name):
        return np.asarray(inputs[name if name.startswith("r_") else "L0_rec_" + name])

    def by_slot(onehot, multi):
        oh = onehot.reshape(BLOCKS, BLOCK, QUARTERS, OH_SLOTS).transpose(2, 1, 0, 3)
        mh = multi.reshape(MULTI, BLOCKS, BLOCK, 2, MH_SLOTS).transpose(0, 3, 2, 1, 4)
        mh = mh.reshape(QUARTERS, BLOCK, BLOCKS, MH_SLOTS)
        return np.ascontiguousarray(np.concatenate([oh, mh], axis=3).reshape(P, BLOCKS * SLOTS))

    def layer(n):
        return np.ascontiguousarray(np.stack([get(f"{m}W{n}").T for m in "QKVR"], axis=1))

    arrays = {
        "idx": by_slot(get("r_onehot_i"), get("r_mh_i")),
        "x": by_slot(get("onehot_x"), get("mh_x")),
        "ctns_t": np.ascontiguousarray(get("ctns").T),
        "xx": np.ascontiguousarray(get("xx")),
        "xy": np.ascontiguousarray(get("xy")),
        "ident": np.eye(P, dtype=np.float32),
        "w1": layer(1),
        "w2": layer(2),
        "bias": np.ascontiguousarray(np.stack([get(f"{m}b{n}") for n in (1, 2) for m in "QKVR"], axis=1)),
        "logit_w": np.ascontiguousarray(get("logitW").reshape(FIELDS, HD).T),
        "logit_b": np.ascontiguousarray(np.broadcast_to(get("logitb"), (P, 1))),
    }
    nc = bacc.Bacc("TRN2", target_bir_lowering=False, num_devices=1)
    aps = {k: nc.dram_tensor(f"in_{k}", v.shape, mybir.dt.from_np(v.dtype), kind="ExternalInput").ap()
           for k, v in arrays.items()}
    out = nc.dram_tensor("out_0", (SAMPLES,), F32, kind="ExternalOutput").ap()
    build(nc, aps, out)
    r = run_bass_kernel_spmd(nc, [{f"in_{k}": v for k, v in arrays.items()}], core_ids=[0])
    return r.results[0]["out_0"]
```

```python
from contextlib import ExitStack

import concourse.bass as bass
from concourse import mybir

F32 = mybir.dt.float32
I32 = mybir.dt.int32
U32 = mybir.dt.uint32
ALU = mybir.AluOpType
ACT = mybir.ActivationFunctionType
AX = mybir.AxisListType

P = 128
SAMPLES = 1024
FIELDS = 32
ONEHOT = 20
MULTI = 2
CONT = 10
BAG = 50
ROWS = 12500
EMB = 64
HD = 128
HEADS = 4
ATT = 32
UNIT = 16
UNITS = SAMPLES // UNIT
BLOCK = 2 * UNIT
BLOCKS = SAMPLES // BLOCK
QUARTERS = 4
OH_SLOTS = ONEHOT // QUARTERS
MH_SLOTS = MULTI * BAG // QUARTERS
SLOTS = OH_SLOTS + MH_SLOTS
CHUNK = SLOTS // 2
COLS = UNIT * FIELDS
GROUP = 4
GROUPS = UNIT // GROUP
GROUP_COLS = GROUP * FIELDS
DMA = 16
LOOP_FIRST = 3
LOOP_UNITS = 4
LOOP_TRIPS = 13


class Unit:

    def __init__(self, base, offset, quarter=None):
        self.base, self.offset, self.quarter_base = base, offset, quarter

    def __add__(self, k):
        return Unit(self.base, self.offset + k, self.quarter_base)

    def number(self):
        return self.offset if self.base is None else self.base + self.offset

    def quarter(self):
        n = self.offset // 4
        return n if self.base is None else self.quarter_base + n

    def mod(self, k):
        return self.offset % k

    def inside(self, first, last):
        return self.base is not None or first <= self.offset <= last


def wait(engine, semaphore, unit, k):
    if unit.base is not None:
        engine.wait_ge(semaphore, unit.base + (unit.offset + k))
    elif unit.offset + k > 0:
        engine.wait_ge(semaphore, unit.offset + k)


def run_units(engine, first, last, one):
    loop_end = LOOP_FIRST + LOOP_UNITS * LOOP_TRIPS
    for n in range(first, LOOP_FIRST):
        one(Unit(None, n))
    with engine.Fori(0, LOOP_TRIPS) as trip:
        base = engine.snap(trip * LOOP_UNITS)
        for r in range(LOOP_UNITS):
            one(Unit(base, LOOP_FIRST + r, trip))
    for n in range(loop_end, last + 1):
        one(Unit(None, n))


def build(nc, a, out):
    with ExitStack() as ctx:
        def sb(name, shape, dt=F32):
            return ctx.enter_context(nc.sbuf_tensor(name, shape, dt))

        def psum(name, shape):
            return ctx.enter_context(nc.psum_tensor(name, shape, F32))

        def sem(name):
            return ctx.enter_context(nc.semaphore(name))

        idx_raw = sb("idx_raw", [P, BLOCKS * SLOTS], I32)
        idx_wrap = sb("idx_wrap", [P, BLOCKS * SLOTS], I32)
        idx_all = sb("idx_all", [P, BLOCKS * SLOTS], I32)
        x_all = sb("x_all", [P, BLOCKS * SLOTS])
        ctns_t = sb("ctns_t", [CONT, SAMPLES])
        xy_wide = sb("xy_wide", [CONT, P])
        ident = sb("ident", [P, P])
        w1 = sb("w1", [P, 4, HD])
        w2 = sb("w2", [P, 4, HD])
        bias = sb("bias", [P, 8])
        out_bias = sb("out_bias", [P, 2])
        logit_w = sb("logit_w", [P, FIELDS])
        logit_b = sb("logit_b", [P, 1])
        neg_logit_b = sb("neg_logit_b", [P, 1])
        ones = sb("ones", [P, 1])
        ctns_diag = sb("ctns_diag", [CONT, SAMPLES * CONT])
        bag_sum = sb("bag_sum", [P, MULTI * BLOCK])

        idx_now = [sb(f"idx_now{b}", [P, SLOTS], I32) for b in range(2)]
        rows = [sb(f"rows{b}", [P, SLOTS, EMB]) for b in range(2)]
        scaled = [sb(f"scaled{b}", [P, SLOTS, EMB]) for b in range(2)]

        y1 = [sb(f"y1_{b}", [P, COLS]) for b in range(2)]
        y2 = [sb(f"y2_{b}", [P, COLS]) for b in range(2)]
        qt = [sb(f"qt{n}", [P, COLS]) for n in range(2)]
        k_diag = [sb(f"k_diag{n}", [P, HEADS * COLS]) for n in range(2)]
        v = [sb(f"v{n}", [P, COLS]) for n in range(2)]
        row_max = [sb(f"row_max{n}", [P, UNIT]) for n in range(2)]
        row_sum = [sb(f"row_sum{n}", [P, UNIT]) for n in range(2)]
        row_inv = [sb(f"row_inv{n}", [P, UNIT]) for n in range(2)]
        shifted = [sb(f"shifted{n}", [P, COLS]) for n in range(2)]
        probs = [sb(f"probs{n}", [P, COLS]) for n in range(2)]
        normed = [sb(f"normed{n}", [P, COLS]) for n in range(2)]
        turned = sb("turned", [P, COLS])
        at_diag = [sb(f"at_diag{n}", [P, GROUP * COLS]) for n in range(2)]
        z = sb("z", [P, COLS])
        weighted = sb("weighted", [P, COLS])
        logit_part = sb("logit_part", [P, SAMPLES])
        expd = sb("expd", [P, SAMPLES // P])
        denom = sb("denom", [P, SAMPLES // P])
        answer = sb("answer", [P, SAMPLES // P])

        ps_y = psum("ps_y", [P, COLS])
        ps_q = psum("ps_q", [P, COLS])
        ps_k = psum("ps_k", [P, COLS])
        ps_v = psum("ps_v", [P, COLS])
        ps_s = [psum(f"ps_s{n}", [P, COLS]) for n in range(2)]
        ps_o = [psum(f"ps_o{n}", [P, COLS]) for n in range(2)]

        idx_loaded = sem("idx_loaded")
        x_loaded = sem("x_loaded")
        const_loaded = sem("const_loaded")
        layer_loaded = sem("layer_loaded")
        idx_step = sem("idx_step")
        idx_ready = sem("idx_ready")
        gathered = [[sem(f"gathered{b}{c}") for c in range(2)] for b in range(2)]
        consts_ready = sem("consts_ready")
        chunk_done = sem("chunk_done")
        y_out = sem("y_out")
        y1_ready = sem("y1_ready")
        q_out = [sem(f"q_out{n}") for n in range(2)]
        k_out = [sem(f"k_out{n}") for n in range(2)]
        v_out = [sem(f"v_out{n}") for n in range(2)]
        q_ready = [sem(f"q_ready{n}") for n in range(2)]
        k_ready = [sem(f"k_ready{n}") for n in range(2)]
        v_ready = [sem(f"v_ready{n}") for n in range(2)]
        scores_out = [sem(f"scores_out{n}") for n in range(2)]
        max_done = [sem(f"max_done{n}") for n in range(2)]
        shift_done = [sem(f"shift_done{n}") for n in range(2)]
        exp_done = [sem(f"exp_done{n}") for n in range(2)]
        sum_done = [sem(f"sum_done{n}") for n in range(2)]
        inv_done = [sem(f"inv_done{n}") for n in range(2)]
        norm_done = [sem(f"norm_done{n}") for n in range(2)]
        turned_ready = sem("turned_ready")
        at_ready = [sem(f"at_ready{n}") for n in range(2)]
        o_out = [sem(f"o_out{n}") for n in range(2)]
        relu_done = [sem(f"relu_done{n}") for n in range(2)]
        weighted_done = sem("weighted_done")
        logit_done = sem("logit_done")
        logits_out = sem("logits_out")
        exp_out = sem("exp_out")
        denom_ready = sem("denom_ready")
        answer_ready = sem("answer_ready")
        stored = sem("stored")
        pe_gate = sem("pe_gate")
        pool_gate = sem("pool_gate")

        def by_key(t):
            return t[:, :].rearrange("p (s k) -> p s k", k=FIELDS)

        def over_keys(t):
            return t[:, :].unsqueeze(2).to_broadcast([P, UNIT, FIELDS])

        block = ctx.enter_context(nc.Block())

        @block.sync
        def _(sp):
            sp.dma_start(idx_raw[:, :], a["idx"]).then_inc(idx_loaded, DMA)
            sp.dma_start(x_all[:, :], a["x"]).then_inc(x_loaded, DMA)
            sp.dma_start(w1[0:EMB, :, :], a["w1"]).then_inc(layer_loaded, DMA)
            sp.dma_start(w2[:, :, :], a["w2"]).then_inc(layer_loaded, DMA)
            sp.dma_start(logit_w[:, :], a["logit_w"]).then_inc(layer_loaded, DMA)
            sp.wait_ge(answer_ready, 1)
            sp.dma_start(out.rearrange("(p n) -> p n", p=P), answer[:, :]).then_inc(stored, DMA)
            sp.wait_ge(stored, DMA)

        @block.gpsimd
        def _(pool):
            def gather_block(parity, n, free):
                for c in range(2):
                    if c == 0:
                        pool.wait_ge(idx_ready, n + 1)
                    if free is not None:
                        pool.wait_ge(chunk_done, free + c)
                    pool.sem_inc(pool_gate, 1)
                    for t in range(c * CHUNK, (c + 1) * CHUNK):
                        pool.indirect_dma_start(
                            rows[parity][:, t, :], None, a["xx"],
                            bass.IndirectOffsetOnAxis(ap=idx_now[parity][:, t:t + 1].bitcast(U32), axis=0),
                        ).then_inc(gathered[parity][c], DMA)

            gather_block(0, 0, None)
            gather_block(1, 1, None)
            with pool.Fori(1, BLOCKS // 2) as pair:
                two = pool.snap(pair * 2)
                four = pool.snap(pair * 4)
                gather_block(0, two, four - 3)
                gather_block(1, two + 1, four - 1)

        @block.tensor
        def _(pe):
            def bags_in(u):
                half = UNIT * u.mod(2)
                parity = u.mod(4) // 2
                pe.wait_ge(chunk_done, (u.quarter() * 4 + 2 * parity) + 2)
                wait(pe, y1_ready, u, 0)
                to = ps_y[0:EMB, :].rearrange("p (s f) -> p f s", f=FIELDS)[:, ONEHOT:ONEHOT + MULTI]
                sums = bag_sum[:, :].rearrange("p (f s) -> p f s", f=MULTI)[:, :, half:half + UNIT]
                for t in range(OH_SLOTS, SLOTS):
                    nc.tensor.matmul(to, scaled[parity][:, t, :], sums, start=t == OH_SLOTS, stop=t == SLOTS - 1)

            def fields_in(u):
                half = UNIT * u.mod(2)
                parity = u.mod(4) // 2
                y = ps_y[:, :].rearrange("p (s f) -> p s f", f=FIELDS)
                first = u.number() * (UNIT * CONT)
                nc.tensor.matmul(y[:, :, ONEHOT + MULTI:],
                                 xy_wide[:, :], ctns_diag[:, bass.ds(first, UNIT * CONT)].rearrange("p (s c) -> p s c", c=CONT),
                                 start=True, stop=True)
                picks = ident[:, :].rearrange("p (q s) -> p q s", s=BLOCK)[:, :, half:half + UNIT]
                for t in range(OH_SLOTS):
                    fields = y[0:EMB, :, t:ONEHOT:OH_SLOTS].rearrange("p s q -> p q s")
                    last = nc.tensor.matmul(fields, scaled[parity][:, t, :], picks, start=True, stop=True)
                last.then_inc(y_out, 1)

            def layer_input(n, u):
                return (y1, y2)[n][u.mod(2)]

            def project(n, u, j):
                nc.tensor.matmul((ps_q, ps_k)[j][:, :], (w1, w2)[n][:, j, :], layer_input(n, u)[:, :],
                                 start=True, stop=True).then_inc((q_out, k_out)[j][n], 1)

            def project_values(n, u):
                for g in range(GROUPS):
                    c = slice(g * GROUP_COLS, (g + 1) * GROUP_COLS)
                    last = nc.tensor.matmul(ps_v[:, c], layer_input(n, u)[:, c], (w1, w2)[n][:, 2, :],
                                            start=True, stop=True)
                last.then_inc(v_out[n], 1)

            def residual(n, u):
                wait(pe, relu_done[n], u, 0)
                nc.tensor.matmul(ps_o[n][:, :], (w1, w2)[n][:, 3, :], layer_input(n, u)[:, :], start=True, stop=False)

            def scores(n, u):
                wait(pe, q_ready[n], u, 1)
                wait(pe, k_ready[n], u, 1)
                wait(pe, shift_done[n], u, 0)
                pe.sem_inc(pe_gate, 1)
                for s in range(UNIT):
                    g, j = divmod(s, GROUP)
                    last = nc.tensor.matmul(ps_s[n][j * FIELDS:(j + 1) * FIELDS, g * HD:(g + 1) * HD],
                                            qt[n][:, s * FIELDS:(s + 1) * FIELDS], k_diag[n][:, s * HD:(s + 1) * HD],
                                            start=True, stop=True, tile_position=(0, j * FIELDS))
                last.then_inc(scores_out[n], 1)

            def attend(n, u):
                wait(pe, v_ready[n], u, 1)
                wait(pe, at_ready[n], u, 1)
                pe.sem_inc(pe_gate, 1)
                for g in range(GROUPS):
                    for h in range(HEADS):
                        r = slice(h * ATT, (h + 1) * ATT)
                        block_cols = (g * HEADS + h) * GROUP_COLS
                        last = nc.tensor.matmul(ps_o[n][r, g * GROUP_COLS:(g + 1) * GROUP_COLS],
                                                v[n][:, g * HD + h * ATT:g * HD + (h + 1) * ATT],
                                                at_diag[n][:, block_cols:block_cols + GROUP_COLS],
                                                start=False, stop=g == GROUPS - 1, tile_position=(0, h * ATT))
                last.then_inc(o_out[n], 1)

            def step(i):
                in_l1 = i.inside(0, UNITS - 1)
                in_l2 = i.inside(1, UNITS)
                leaves = i.inside(2, UNITS + 1)
                enters = i.inside(-1, UNITS - 2)
                if enters:
                    bags_in(i + 1)
                if leaves:
                    residual(1, i + -2)
                if in_l1:
                    scores(0, i)
                if leaves:
                    attend(1, i + -2)
                if in_l2:
                    wait(pe, relu_done[0], i, 0)
                    project(1, i + -1, 1)
                    project(1, i + -1, 0)
                    if in_l1:
                        wait(pe, v_ready[0], i, 1)
                    else:
                        wait(pe, v_ready[1], i, -1)
                    project_values(1, i + -1)
                if enters:
                    fields_in(i + 1)
                if in_l1:
                    residual(0, i)
                if in_l2:
                    scores(1, i + -1)
                if in_l1:
                    attend(0, i)
                if enters:
                    wait(pe, y1_ready, i, 2)
                    project(0, i + 1, 1)
                    project(0, i + 1, 0)
                    if in_l2:
                        wait(pe, v_ready[1], i, 0)
                    else:
                        wait(pe, v_ready[0], i, 1)
                    project_values(0, i + 1)

            pe.wait_ge(layer_loaded, 3 * DMA)
            pe.wait_ge(const_loaded, 5 * DMA)
            pe.wait_ge(consts_ready, 13)
            run_units(pe, -1, UNITS + 1, step)

            pe.wait_ge(logit_done, UNITS)
            per = SAMPLES // P
            part = logit_part[:, :].rearrange("c (p n) -> c n p", n=per)
            for n in range(per):
                last = nc.tensor.matmul(ps_y[:, n:n + 1], part[:, n, :], ones[:, :], start=True, stop=True)
            last.then_inc(logits_out, 1)

        @block.scalar
        def _(act):
            act.dma_start(ident[:, :], a["ident"]).then_inc(const_loaded, DMA)
            act.dma_start(ctns_t[:, :], a["ctns_t"]).then_inc(const_loaded, DMA)
            act.dma_start(xy_wide[:, 0:EMB], a["xy"]).then_inc(const_loaded, DMA)
            act.dma_start(bias[:, :], a["bias"]).then_inc(const_loaded, DMA)
            act.dma_start(logit_b[:, :], a["logit_b"]).then_inc(const_loaded, DMA)

            def queries(n, u):
                wait(act, q_out[n], u, 1)
                nc.scalar.activation(qt[n][:, :], ps_q[:, :], ACT.Identity,
                                     bias=bias[:, 4 * n:4 * n + 1]).then_inc(q_ready[n], 1)

            def keys(n, u):
                wait(act, k_out[n], u, 1)
                for h in range(HEADS):
                    r = slice(h * ATT, (h + 1) * ATT)
                    to = k_diag[n][r, :].rearrange("p (s h k) -> p s h k", h=HEADS, k=FIELDS)[:, :, h]
                    last = nc.scalar.activation(to, by_key(ps_k)[r], ACT.Identity,
                                                bias=bias[r, 4 * n + 1:4 * n + 2])
                last.then_inc(k_ready[n], 1)

            def values(n, u):
                wait(act, v_out[n], u, 1)
                nc.scalar.activation(v[n][:, :], ps_v[:, :], ACT.Copy).then_inc(v_ready[n], 1)

            def exponential(n, u):
                wait(act, shift_done[n], u, 1)
                wait(act, norm_done[n], u, 0)
                nc.scalar.activation(probs[n][:, :], shifted[n][:, :], ACT.Exp).then_inc(exp_done[n], 1)

            def spread(u):
                wait(act, turned_ready, u, 1)
                wait(act, o_out[1], u, 0)
                for j in range(GROUP):
                    r = slice(j * FIELDS, (j + 1) * FIELDS)
                    to = at_diag[1][r, :].rearrange("p (b j q) -> p b j q", j=GROUP, q=FIELDS)[:, :, j]
                    last = nc.scalar.activation(to, by_key(turned)[r], ACT.Copy)
                last.then_inc(at_ready[1], 1)

            def relu(n, u, y):
                wait(act, o_out[n], u, 1)
                nc.scalar.activation(y[:, :], ps_o[n][:, :], ACT.Relu,
                                     bias=out_bias[:, n:n + 1]).then_inc(relu_done[n], 1)

            def step(i):
                in_l1 = i.inside(0, UNITS - 1)
                in_l2 = i.inside(1, UNITS)
                leaves = i.inside(2, UNITS + 1)
                enters = i.inside(-1, UNITS - 2)
                if leaves:
                    spread(i + -2)
                if in_l1:
                    exponential(0, i)
                if leaves:
                    wait(act, weighted_done, i, -2)
                    relu(1, i + -2, z)
                if in_l2:
                    keys(1, i + -1)
                    queries(1, i + -1)
                    values(1, i + -1)
                if enters:
                    u = i + 1
                    wait(act, y_out, u, 1)
                    wait(act, o_out[0], i, 0)
                    nc.scalar.activation(y1[u.mod(2)][0:EMB, :], ps_y[0:EMB, :], ACT.Copy).then_inc(y1_ready, 1)
                if in_l1:
                    wait(act, o_out[1], i, -1)
                    relu(0, i, y2[i.mod(2)])
                if in_l2:
                    exponential(1, i + -1)
                if enters:
                    keys(0, i + 1)
                    queries(0, i + 1)
                    values(0, i + 1)

            act.wait_ge(const_loaded, 5 * DMA)
            act.wait_ge(consts_ready, 13)
            run_units(act, -1, UNITS + 1, step)

            act.wait_ge(logits_out, 1)
            nc.scalar.activation(expd[:, :], ps_y[:, 0:SAMPLES // P], ACT.Exp, scale=-1.0,
                                 bias=neg_logit_b[:, :]).then_inc(exp_out, 1)

        @block.vector
        def _(dve):
            def wrap_indices(lo, hi, count):
                c = slice(lo * SLOTS, hi * SLOTS)
                nc.vector.tensor_scalar(idx_wrap[:, c], idx_raw[:, c], 0.0, float(ROWS),
                                        ALU.is_lt, ALU.mult).then_inc(idx_step, 1)
                dve.wait_ge(idx_step, count + 1)
                nc.vector.tensor_tensor(idx_wrap[:, c], idx_raw[:, c], idx_wrap[:, c], ALU.add).then_inc(idx_step, 1)
                dve.wait_ge(idx_step, count + 2)
                nc.vector.tensor_scalar(idx_all[:, c], idx_wrap[:, c], 0.0, float(ROWS - 1),
                                        ALU.max, ALU.min).then_inc(idx_step, 1)
                dve.wait_ge(idx_step, count + 3)

            def chunk(m):
                c = m.mod(2)
                parity = m.mod(4) // 2
                half_block = m.quarter()
                dve.wait_ge(gathered[parity][c], (half_block + 1) * (DMA * CHUNK))
                wait(dve, y_out, m, -2 - c)
                first = (half_block * 2 + parity) * SLOTS
                slots = slice(c * CHUNK, (c + 1) * CHUNK)
                nc.vector.tensor_tensor(
                    scaled[parity][:, slots, :], rows[parity][:, slots, :],
                    x_all[:, bass.ds(first + c * CHUNK, CHUNK)].unsqueeze(2).to_broadcast([P, CHUNK, EMB]),
                    ALU.mult).then_inc(chunk_done, 1)
                if c == 1 and m.inside(0, UNITS - 5):
                    nc.vector.tensor_copy(
                        idx_now[parity][:, :],
                        idx_all[:, bass.ds(first + 2 * SLOTS, SLOTS)]).then_inc(idx_ready, 1)

            def shift(n, u):
                wait(dve, scores_out[n], u, 1)
                nc.vector.tensor_reduce(row_max[n][:, :], by_key(ps_s[n]), AX.X, ALU.max).then_inc(max_done[n], 1)
                wait(dve, max_done[n], u, 1)
                wait(dve, exp_done[n], u, 0)
                nc.vector.tensor_tensor(by_key(shifted[n]), by_key(ps_s[n]), over_keys(row_max[n]),
                                        ALU.subtract).then_inc(shift_done[n], 1)

            def normalise(n, u):
                wait(dve, exp_done[n], u, 1)
                nc.vector.tensor_reduce(row_sum[n][:, :], by_key(probs[n]), AX.X, ALU.add).then_inc(sum_done[n], 1)
                wait(dve, sum_done[n], u, 1)
                nc.vector.reciprocal(row_inv[n][:, :], row_sum[n][:, :]).then_inc(inv_done[n], 1)
                wait(dve, inv_done[n], u, 1)
                nc.vector.tensor_tensor(by_key(normed[n]), by_key(probs[n]), over_keys(row_inv[n]),
                                        ALU.mult).then_inc(norm_done[n], 1)
                wait(dve, norm_done[n], u, 1)
                if n == 1:
                    wait(dve, at_ready[1], u, 0)
                    nc.vector.transpose(turned[:, :], normed[n][:, :]).then_inc(turned_ready, 1)
                    return
                wait(dve, o_out[n], u, 0)
                for j in range(GROUP):
                    r = slice(j * FIELDS, (j + 1) * FIELDS)
                    to = at_diag[n][r, :].rearrange("p (b j q) -> p b j q", j=GROUP, q=FIELDS)[:, :, j]
                    last = nc.vector.transpose(to, by_key(normed[n])[r])
                last.then_inc(at_ready[n], 1)

            def logit(u):
                wait(dve, relu_done[1], u, 1)
                nc.vector.tensor_tensor(
                    by_key(weighted), by_key(z), logit_w[:, :].unsqueeze(1).to_broadcast([P, UNIT, FIELDS]),
                    ALU.mult).then_inc(weighted_done, 1)
                wait(dve, weighted_done, u, 1)
                nc.vector.tensor_reduce(logit_part[:, bass.ds(u.number() * UNIT, UNIT)], by_key(weighted), AX.X,
                                        ALU.add).then_inc(logit_done, 1)

            def step(i):
                if i.inside(0, UNITS - 1):
                    shift(0, i)
                if i.inside(-1, UNITS - 4):
                    chunk(i + 3)
                if i.inside(0, UNITS - 1):
                    normalise(0, i)
                if i.inside(2, UNITS + 1):
                    logit(i + -2)
                if i.inside(1, UNITS):
                    shift(1, i + -1)
                    normalise(1, i + -1)

            dve.wait_ge(idx_loaded, DMA)
            wrap_indices(0, 2, 0)
            for b in range(2):
                nc.vector.tensor_copy(idx_now[b][:, :], idx_all[:, b * SLOTS:(b + 1) * SLOTS]).then_inc(idx_ready, 1)
            wrap_indices(2, BLOCKS, 3)
            nc.vector.memset(xy_wide[:, EMB:P], 0.0).then_inc(consts_ready, 1)
            nc.vector.memset(ones[:, :], 1.0).then_inc(consts_ready, 1)
            for b in range(2):
                nc.vector.memset(y1[b][EMB:P, :], 0.0).then_inc(consts_ready, 1)
            nc.vector.memset(w1[EMB:P, :, :], 0.0).then_inc(consts_ready, 1)
            for n in range(2):
                nc.vector.memset(k_diag[n][:, :], 0.0).then_inc(consts_ready, 1)
                nc.vector.memset(at_diag[n][:, :], 0.0).then_inc(consts_ready, 1)
            dve.wait_ge(const_loaded, 5 * DMA)
            nc.vector.tensor_tensor(out_bias[:, :], bias[:, 2::4], bias[:, 3::4], ALU.add).then_inc(consts_ready, 1)
            nc.vector.tensor_tensor(
                ctns_diag[:, :].rearrange("p (s c) -> p s c", c=CONT),
                ctns_t[:, :].unsqueeze(2).to_broadcast([CONT, SAMPLES, CONT]),
                ident[0:CONT, 0:CONT].unsqueeze(1).to_broadcast([CONT, SAMPLES, CONT]),
                ALU.mult).then_inc(consts_ready, 1)
            halves = ident[:, :].rearrange("p (f h s) -> p h f s", f=MULTI, h=2)
            nc.vector.tensor_tensor(bag_sum[:, :].rearrange("p (f s) -> p f s", f=MULTI),
                                    halves[:, 0], halves[:, 1], ALU.add).then_inc(consts_ready, 1)
            nc.vector.tensor_scalar(neg_logit_b[:, :], logit_b[:, :], -1.0, None, ALU.mult).then_inc(consts_ready, 1)
            dve.wait_ge(layer_loaded, 3 * DMA)
            dve.wait_ge(x_loaded, DMA)
            chunk(Unit(None, 0))
            chunk(Unit(None, 1))
            run_units(dve, -1, UNITS + 1, step)

            dve.wait_ge(exp_out, 1)
            nc.vector.tensor_scalar(denom[:, :], expd[:, :], 1.0, None, ALU.add).then_inc(denom_ready, 1)
            dve.wait_ge(denom_ready, 1)
            nc.vector.reciprocal(answer[:, :], denom[:, :]).then_inc(answer_ready, 1)


def kernel(**inputs):
    import numpy as np
    import concourse.bacc as bacc
    from concourse.bass_utils import run_bass_kernel_spmd

    def get(name):
        return np.asarray(inputs[name if name.startswith("r_") else "L0_rec_" + name])

    def by_slot(onehot, multi):
        oh = onehot.reshape(BLOCKS, BLOCK, QUARTERS, OH_SLOTS).transpose(2, 1, 0, 3)
        mh = multi.reshape(MULTI, BLOCKS, BLOCK, 2, MH_SLOTS).transpose(0, 3, 2, 1, 4)
        mh = mh.reshape(QUARTERS, BLOCK, BLOCKS, MH_SLOTS)
        return np.ascontiguousarray(np.concatenate([oh, mh], axis=3).reshape(P, BLOCKS * SLOTS))

    def layer(n):
        return np.ascontiguousarray(np.stack([get(f"{m}W{n}").T for m in "QKVR"], axis=1))

    arrays = {
        "idx": by_slot(get("r_onehot_i"), get("r_mh_i")),
        "x": by_slot(get("onehot_x"), get("mh_x")),
        "ctns_t": np.ascontiguousarray(get("ctns").T),
        "xx": np.ascontiguousarray(get("xx")),
        "xy": np.ascontiguousarray(get("xy")),
        "ident": np.eye(P, dtype=np.float32),
        "w1": layer(1),
        "w2": layer(2),
        "bias": np.ascontiguousarray(np.stack([get(f"{m}b{n}") for n in (1, 2) for m in "QKVR"], axis=1)),
        "logit_w": np.ascontiguousarray(get("logitW").reshape(FIELDS, HD).T),
        "logit_b": np.ascontiguousarray(np.broadcast_to(get("logitb"), (P, 1))),
    }
    nc = bacc.Bacc("TRN2", target_bir_lowering=False, num_devices=1)
    aps = {k: nc.dram_tensor(f"in_{k}", v.shape, mybir.dt.from_np(v.dtype), kind="ExternalInput").ap()
           for k, v in arrays.items()}
    out = nc.dram_tensor("out_0", (SAMPLES,), F32, kind="ExternalOutput").ap()
    build(nc, aps, out)
    r = run_bass_kernel_spmd(nc, [{f"in_{k}": v for k, v in arrays.items()}], core_ids=[0])
    return r.results[0]["out_0"]
```

```python
from contextlib import ExitStack

import concourse.bass as bass
from concourse import mybir

F32 = mybir.dt.float32
I32 = mybir.dt.int32
U32 = mybir.dt.uint32
ALU = mybir.AluOpType
ACT = mybir.ActivationFunctionType
AX = mybir.AxisListType

P = 128
SAMPLES = 1024
FIELDS = 32
ONEHOT = 20
MULTI = 2
CONT = 10
BAG = 50
ROWS = 12500
EMB = 64
HD = 128
HEADS = 4
ATT = 32
UNIT = 16
UNITS = SAMPLES // UNIT
BLOCK = 2 * UNIT
BLOCKS = SAMPLES // BLOCK
QUARTERS = 4
OH_SLOTS = ONEHOT // QUARTERS
MH_SLOTS = MULTI * BAG // QUARTERS
SLOTS = OH_SLOTS + MH_SLOTS
CHUNK = SLOTS // 2
FOLD = MH_SLOTS // 2
BAG_SLOTS = (*range(OH_SLOTS, OH_SLOTS + FOLD), *range(OH_SLOTS + 2 * FOLD, SLOTS))
COLS = UNIT * FIELDS
GROUP = 4
GROUPS = UNIT // GROUP
GROUP_COLS = GROUP * FIELDS
OUT_COLS = SAMPLES // P
EARLY = (0, SAMPLES - BLOCK, 0)
LATE = (SAMPLES - BLOCK, BLOCK, OUT_COLS)
DMA = 16
LOOP_FIRST = 3
LOOP_UNITS = 4
LOOP_TRIPS = 13


class Unit:

    def __init__(self, base, offset, quarter=None):
        self.base, self.offset, self.quarter_base = base, offset, quarter

    def __add__(self, k):
        return Unit(self.base, self.offset + k, self.quarter_base)

    def number(self):
        return self.offset if self.base is None else self.base + self.offset

    def quarter(self):
        n = self.offset // 4
        return n if self.base is None else self.quarter_base + n

    def mod(self, k):
        return self.offset % k

    def inside(self, first, last):
        return self.base is not None or first <= self.offset <= last

    def is_number(self, n):
        return self.base is None and self.offset == n


def wait(engine, semaphore, unit, k):
    if unit.base is not None:
        engine.wait_ge(semaphore, unit.base + (unit.offset + k))
    elif unit.offset + k > 0:
        engine.wait_ge(semaphore, unit.offset + k)


def run_units(engine, first, last, one):
    loop_end = LOOP_FIRST + LOOP_UNITS * LOOP_TRIPS
    for n in range(first, LOOP_FIRST):
        one(Unit(None, n))
    with engine.Fori(0, LOOP_TRIPS) as trip:
        base = engine.snap(trip * LOOP_UNITS)
        for r in range(LOOP_UNITS):
            one(Unit(base, LOOP_FIRST + r, trip))
    for n in range(loop_end, last + 1):
        one(Unit(None, n))


def build(nc, a, out):
    with ExitStack() as ctx:
        def sb(name, shape, dt=F32):
            return ctx.enter_context(nc.sbuf_tensor(name, shape, dt))

        def psum(name, shape):
            return ctx.enter_context(nc.psum_tensor(name, shape, F32))

        def sem(name):
            return ctx.enter_context(nc.semaphore(name))

        idx_raw = sb("idx_raw", [P, BLOCKS * SLOTS], I32)
        idx_wrap = sb("idx_wrap", [P, BLOCKS * SLOTS], I32)
        idx_all = sb("idx_all", [P, BLOCKS * SLOTS], I32)
        x_all = sb("x_all", [P, BLOCKS * SLOTS])
        ctns_t = sb("ctns_t", [CONT, SAMPLES])
        xy_wide = sb("xy_wide", [CONT, P])
        ident = sb("ident", [P, P])
        w1 = sb("w1", [P, 4, HD])
        w2 = sb("w2", [P, 4, HD])
        bias = sb("bias", [P, 8])
        out_bias = sb("out_bias", [P, 2])
        logit_w = sb("logit_w", [P, FIELDS])
        logit_b = sb("logit_b", [P, 1])
        neg_logit_b = sb("neg_logit_b", [P, 1])
        ones = sb("ones", [P, 1])
        ctns_diag = sb("ctns_diag", [CONT, SAMPLES * CONT])
        bag_sum = sb("bag_sum", [P, MULTI * BLOCK])

        idx_now = [sb(f"idx_now{b}", [P, SLOTS], I32) for b in range(2)]
        rows = [sb(f"rows{b}", [P, SLOTS, EMB]) for b in range(2)]
        scaled = [sb(f"scaled{b}", [P, SLOTS, EMB]) for b in range(2)]

        y1 = [sb(f"y1_{b}", [P, COLS]) for b in range(2)]
        y2 = [sb(f"y2_{b}", [P, COLS]) for b in range(2)]
        qt = [sb(f"qt{n}", [P, COLS]) for n in range(2)]
        k_diag = [sb(f"k_diag{n}", [P, HEADS * COLS]) for n in range(2)]
        v = [sb(f"v{n}", [P, COLS]) for n in range(2)]
        row_max = [sb(f"row_max{n}", [P, UNIT]) for n in range(2)]
        row_sum = [sb(f"row_sum{n}", [P, UNIT]) for n in range(2)]
        row_inv = [sb(f"row_inv{n}", [P, UNIT]) for n in range(2)]
        shifted = [sb(f"shifted{n}", [P, COLS]) for n in range(2)]
        probs = [sb(f"probs{n}", [P, COLS]) for n in range(2)]
        normed = [sb(f"normed{n}", [P, COLS]) for n in range(2)]
        turned = sb("turned", [P, COLS])
        at_diag = [sb(f"at_diag{n}", [P, GROUP * COLS]) for n in range(2)]
        z = sb("z", [P, COLS])
        weighted = sb("weighted", [P, COLS])
        logit_part = sb("logit_part", [P, SAMPLES])
        expd = sb("expd", [P, 2 * OUT_COLS])
        denom = sb("denom", [P, 2 * OUT_COLS])
        answer = sb("answer", [P, 2 * OUT_COLS])

        ps_y = psum("ps_y", [P, COLS])
        ps_q = psum("ps_q", [P, COLS])
        ps_k = psum("ps_k", [P, COLS])
        ps_v = psum("ps_v", [P, COLS])
        ps_s = [psum(f"ps_s{n}", [P, COLS]) for n in range(2)]
        ps_o = [psum(f"ps_o{n}", [P, COLS]) for n in range(2)]

        idx_loaded = sem("idx_loaded")
        x_loaded = sem("x_loaded")
        const_loaded = sem("const_loaded")
        layer_loaded = sem("layer_loaded")
        idx_step = sem("idx_step")
        idx_ready = sem("idx_ready")
        gathered = [[sem(f"gathered{b}{c}") for c in range(2)] for b in range(2)]
        consts_ready = sem("consts_ready")
        chunk_done = sem("chunk_done")
        bag_folded = sem("bag_folded")
        y_out = sem("y_out")
        y1_ready = sem("y1_ready")
        q_out = [sem(f"q_out{n}") for n in range(2)]
        k_out = [sem(f"k_out{n}") for n in range(2)]
        v_out = [sem(f"v_out{n}") for n in range(2)]
        q_ready = [sem(f"q_ready{n}") for n in range(2)]
        k_ready = [sem(f"k_ready{n}") for n in range(2)]
        v_ready = [sem(f"v_ready{n}") for n in range(2)]
        scores_out = [sem(f"scores_out{n}") for n in range(2)]
        max_done = [sem(f"max_done{n}") for n in range(2)]
        shift_done = [sem(f"shift_done{n}") for n in range(2)]
        exp_done = [sem(f"exp_done{n}") for n in range(2)]
        sum_done = [sem(f"sum_done{n}") for n in range(2)]
        inv_done = [sem(f"inv_done{n}") for n in range(2)]
        norm_done = [sem(f"norm_done{n}") for n in range(2)]
        turned_ready = sem("turned_ready")
        at_ready = [sem(f"at_ready{n}") for n in range(2)]
        o_out = [sem(f"o_out{n}") for n in range(2)]
        relu_done = [sem(f"relu_done{n}") for n in range(2)]
        weighted_done = sem("weighted_done")
        logit_done = sem("logit_done")
        logits_out = sem("logits_out")
        exp_out = sem("exp_out")
        denom_ready = sem("denom_ready")
        answer_ready = sem("answer_ready")
        stored = sem("stored")
        pe_gate = sem("pe_gate")
        pool_gate = sem("pool_gate")

        def by_key(t):
            return t[:, :].rearrange("p (s k) -> p s k", k=FIELDS)

        def over_keys(t):
            return t[:, :].unsqueeze(2).to_broadcast([P, UNIT, FIELDS])

        def of_part(t, part):
            return t[0:part[1] // OUT_COLS, part[2]:part[2] + OUT_COLS]

        block = ctx.enter_context(nc.Block())

        @block.sync
        def _(sp):
            sp.dma_start(idx_raw[:, :], a["idx"]).then_inc(idx_loaded, DMA)
            sp.dma_start(x_all[:, :], a["x"]).then_inc(x_loaded, DMA)
            sp.dma_start(w1[0:EMB, :, :], a["w1"]).then_inc(layer_loaded, DMA)
            sp.dma_start(w2[:, :, :], a["w2"]).then_inc(layer_loaded, DMA)
            sp.dma_start(logit_w[:, :], a["logit_w"]).then_inc(layer_loaded, DMA)
            for n, part in enumerate((EARLY, LATE)):
                sp.wait_ge(answer_ready, n + 1)
                first, count, _ = part
                sp.dma_start(out[first:first + count].rearrange("(p n) -> p n", n=OUT_COLS),
                             of_part(answer, part)).then_inc(stored, DMA)
            sp.wait_ge(stored, 2 * DMA)

        @block.gpsimd
        def _(pool):
            def gather_block(parity, n, free):
                for c in range(2):
                    if c == 0:
                        pool.wait_ge(idx_ready, n + 1)
                    if free is not None:
                        pool.wait_ge(chunk_done, free + c)
                    pool.sem_inc(pool_gate, 1)
                    for t in range(c * CHUNK, (c + 1) * CHUNK):
                        pool.indirect_dma_start(
                            rows[parity][:, t, :], None, a["xx"],
                            bass.IndirectOffsetOnAxis(ap=idx_now[parity][:, t:t + 1].bitcast(U32), axis=0),
                        ).then_inc(gathered[parity][c], DMA)

            gather_block(0, 0, None)
            gather_block(1, 1, None)
            with pool.Fori(1, BLOCKS // 2) as pair:
                two = pool.snap(pair * 2)
                four = pool.snap(pair * 4)
                gather_block(0, two, four - 3)
                gather_block(1, two + 1, four - 1)

        @block.tensor
        def _(pe):
            def bags_in(u):
                half = UNIT * u.mod(2)
                parity = u.mod(4) // 2
                to = ps_y[0:EMB, :].rearrange("p (s f) -> p f s", f=FIELDS)[:, ONEHOT:ONEHOT + MULTI]
                sums = bag_sum[:, :].rearrange("p (f s) -> p f s", f=MULTI)[:, :, half:half + UNIT]
                for t in BAG_SLOTS:
                    last = nc.tensor.matmul(to, scaled[parity][:, t, :], sums, start=t == BAG_SLOTS[0],
                                            stop=t == BAG_SLOTS[-1])
                last.then_inc(y_out, 1)

            def fields_in(u):
                half = UNIT * u.mod(2)
                parity = u.mod(4) // 2
                pe.wait_ge(bag_folded, (u.quarter() * 2 + parity) + 1)
                wait(pe, y1_ready, u, 0)
                y = ps_y[:, :].rearrange("p (s f) -> p s f", f=FIELDS)
                first = u.number() * (UNIT * CONT)
                nc.tensor.matmul(y[:, :, ONEHOT + MULTI:],
                                 xy_wide[:, :],
                                 ctns_diag[:, bass.ds(first, UNIT * CONT)].rearrange("p (s c) -> p s c", c=CONT),
                                 start=True, stop=True)
                picks = ident[:, :].rearrange("p (q s) -> p q s", s=BLOCK)[:, :, half:half + UNIT]
                for t in range(OH_SLOTS):
                    fields = y[0:EMB, :, t:ONEHOT:OH_SLOTS].rearrange("p s q -> p q s")
                    nc.tensor.matmul(fields, scaled[parity][:, t, :], picks, start=True, stop=True)

            def layer_input(n, u):
                return (y1, y2)[n][u.mod(2)]

            def project(n, u, j):
                nc.tensor.matmul((ps_q, ps_k)[j][:, :], (w1, w2)[n][:, j, :], layer_input(n, u)[:, :],
                                 start=True, stop=True).then_inc((q_out, k_out)[j][n], 1)

            def project_values(n, u):
                for g in range(GROUPS):
                    c = slice(g * GROUP_COLS, (g + 1) * GROUP_COLS)
                    last = nc.tensor.matmul(ps_v[:, c], layer_input(n, u)[:, c], (w1, w2)[n][:, 2, :],
                                            start=True, stop=True)
                last.then_inc(v_out[n], 1)

            def residual(n, u):
                wait(pe, relu_done[n], u, 0)
                nc.tensor.matmul(ps_o[n][:, :], (w1, w2)[n][:, 3, :], layer_input(n, u)[:, :], start=True, stop=False)

            def scores(n, u):
                wait(pe, q_ready[n], u, 1)
                wait(pe, k_ready[n], u, 1)
                wait(pe, shift_done[n], u, 0)
                pe.sem_inc(pe_gate, 1)
                for s in range(UNIT):
                    g, j = divmod(s, GROUP)
                    last = nc.tensor.matmul(ps_s[n][j * FIELDS:(j + 1) * FIELDS, g * HD:(g + 1) * HD],
                                            qt[n][:, s * FIELDS:(s + 1) * FIELDS], k_diag[n][:, s * HD:(s + 1) * HD],
                                            start=True, stop=True, tile_position=(0, j * FIELDS))
                last.then_inc(scores_out[n], 1)

            def attend(n, u):
                wait(pe, v_ready[n], u, 1)
                wait(pe, at_ready[n], u, 1)
                pe.sem_inc(pe_gate, 1)
                for g in range(GROUPS):
                    for h in range(HEADS):
                        r = slice(h * ATT, (h + 1) * ATT)
                        block_cols = (g * HEADS + h) * GROUP_COLS
                        last = nc.tensor.matmul(ps_o[n][r, g * GROUP_COLS:(g + 1) * GROUP_COLS],
                                                v[n][:, g * HD + h * ATT:g * HD + (h + 1) * ATT],
                                                at_diag[n][:, block_cols:block_cols + GROUP_COLS],
                                                start=False, stop=g == GROUPS - 1, tile_position=(0, h * ATT))
                last.then_inc(o_out[n], 1)

            def sum_channels(part, units):
                first, count, to = part
                pe.wait_ge(logit_done, units)
                weights = logit_part[:, first:first + count].rearrange("c (p n) -> c n p", n=OUT_COLS)
                for n in range(OUT_COLS):
                    last = nc.tensor.matmul(ps_y[0:count // OUT_COLS, to + n:to + n + 1], weights[:, n, :], ones[:, :],
                                            start=True, stop=True)
                last.then_inc(logits_out, 1)

            def step(i):
                in_l1 = i.inside(0, UNITS - 1)
                in_l2 = i.inside(1, UNITS)
                leaves = i.inside(2, UNITS + 1)
                enters = i.inside(-1, UNITS - 2)
                if leaves:
                    residual(1, i + -2)
                if in_l1:
                    scores(0, i)
                if i.is_number(UNITS):
                    wait(pe, relu_done[0], i, 0)
                    project(1, i + -1, 1)
                    project(1, i + -1, 0)
                    sum_channels(EARLY, UNITS - BLOCK // UNIT)
                    scores(1, i + -1)
                    wait(pe, v_ready[1], i, -1)
                    project_values(1, i + -1)
                    attend(1, i + -2)
                    return
                if leaves:
                    attend(1, i + -2)
                if in_l2:
                    wait(pe, relu_done[0], i, 0)
                    project(1, i + -1, 1)
                    project(1, i + -1, 0)
                    wait(pe, v_ready[0], i, 1)
                    project_values(1, i + -1)
                if enters:
                    fields_in(i + 1)
                if in_l1:
                    residual(0, i)
                if in_l2:
                    scores(1, i + -1)
                if enters:
                    bags_in(i + 1)
                if in_l1:
                    attend(0, i)
                if enters:
                    wait(pe, y1_ready, i, 2)
                    project(0, i + 1, 1)
                    project(0, i + 1, 0)
                    if in_l2:
                        wait(pe, v_ready[1], i, 0)
                    else:
                        wait(pe, v_ready[0], i, 1)
                    project_values(0, i + 1)

            pe.wait_ge(layer_loaded, 3 * DMA)
            pe.wait_ge(const_loaded, 5 * DMA)
            pe.wait_ge(consts_ready, 13)
            run_units(pe, -1, UNITS + 1, step)

            sum_channels(LATE, UNITS)

        @block.scalar
        def _(act):
            act.dma_start(ident[:, :], a["ident"]).then_inc(const_loaded, DMA)
            act.dma_start(ctns_t[:, :], a["ctns_t"]).then_inc(const_loaded, DMA)
            act.dma_start(xy_wide[:, 0:EMB], a["xy"]).then_inc(const_loaded, DMA)
            act.dma_start(bias[:, :], a["bias"]).then_inc(const_loaded, DMA)
            act.dma_start(logit_b[:, :], a["logit_b"]).then_inc(const_loaded, DMA)

            def queries(u):
                wait(act, q_out[1], u, 1)
                nc.scalar.activation(qt[1][:, :], ps_q[:, :], ACT.Identity,
                                     bias=bias[:, 4:5]).then_inc(q_ready[1], 1)

            def keys(n, u):
                wait(act, k_out[n], u, 1)
                for h in range(HEADS):
                    r = slice(h * ATT, (h + 1) * ATT)
                    to = k_diag[n][r, :].rearrange("p (s h k) -> p s h k", h=HEADS, k=FIELDS)[:, :, h]
                    last = nc.scalar.activation(to, by_key(ps_k)[r], ACT.Identity,
                                                bias=bias[r, 4 * n + 1:4 * n + 2])
                last.then_inc(k_ready[n], 1)

            def values(n, u):
                wait(act, v_out[n], u, 1)
                nc.scalar.activation(v[n][:, :], ps_v[:, :], ACT.Copy).then_inc(v_ready[n], 1)

            def exponential(n, u):
                wait(act, shift_done[n], u, 1)
                wait(act, norm_done[n], u, 0)
                nc.scalar.activation(probs[n][:, :], shifted[n][:, :], ACT.Exp).then_inc(exp_done[n], 1)

            def sigmoid_exp(n, part):
                act.wait_ge(logits_out, n + 1)
                nc.scalar.activation(of_part(expd, part), of_part(ps_y, part), ACT.Exp, scale=-1.0,
                                     bias=neg_logit_b[0:part[1] // OUT_COLS, :]).then_inc(exp_out, 1)

            def spread(u):
                wait(act, turned_ready, u, 1)
                wait(act, o_out[1], u, 0)
                for j in range(GROUP):
                    r = slice(j * FIELDS, (j + 1) * FIELDS)
                    to = at_diag[1][r, :].rearrange("p (b j q) -> p b j q", j=GROUP, q=FIELDS)[:, :, j]
                    last = nc.scalar.activation(to, by_key(turned)[r], ACT.Copy)
                last.then_inc(at_ready[1], 1)

            def relu(n, u, y):
                wait(act, o_out[n], u, 1)
                nc.scalar.activation(y[:, :], ps_o[n][:, :], ACT.Relu,
                                     bias=out_bias[:, n:n + 1]).then_inc(relu_done[n], 1)

            def step(i):
                in_l1 = i.inside(0, UNITS - 1)
                in_l2 = i.inside(1, UNITS)
                leaves = i.inside(2, UNITS + 1)
                enters = i.inside(-1, UNITS - 2)
                if i.is_number(UNITS):
                    keys(1, i + -1)
                    queries(i + -1)
                    spread(i + -2)
                    exponential(1, i + -1)
                    wait(act, weighted_done, i, -2)
                    relu(1, i + -2, z)
                    values(1, i + -1)
                    sigmoid_exp(0, EARLY)
                    return
                if leaves:
                    spread(i + -2)
                if in_l1:
                    values(0, i)
                if in_l1:
                    exponential(0, i)
                if leaves:
                    wait(act, weighted_done, i, -2)
                    relu(1, i + -2, z)
                if in_l2:
                    keys(1, i + -1)
                    queries(i + -1)
                    values(1, i + -1)
                if enters:
                    u = i + 1
                    wait(act, y_out, u, 1)
                    wait(act, o_out[0], i, 0)
                    nc.scalar.activation(y1[u.mod(2)][0:EMB, :], ps_y[0:EMB, :], ACT.Copy).then_inc(y1_ready, 1)
                if in_l2:
                    exponential(1, i + -1)
                if in_l1:
                    wait(act, o_out[1], i, -1)
                    relu(0, i, y2[i.mod(2)])
                if enters:
                    keys(0, i + 1)

            act.wait_ge(const_loaded, 5 * DMA)
            act.wait_ge(consts_ready, 13)
            run_units(act, -1, UNITS + 1, step)

            sigmoid_exp(1, LATE)

        @block.vector
        def _(dve):
            def wrap_indices(lo, hi, count):
                c = slice(lo * SLOTS, hi * SLOTS)
                nc.vector.tensor_scalar(idx_wrap[:, c], idx_raw[:, c], 0.0, float(ROWS),
                                        ALU.is_lt, ALU.mult).then_inc(idx_step, 1)
                dve.wait_ge(idx_step, count + 1)
                nc.vector.tensor_tensor(idx_wrap[:, c], idx_raw[:, c], idx_wrap[:, c], ALU.add).then_inc(idx_step, 1)
                dve.wait_ge(idx_step, count + 2)
                nc.vector.tensor_scalar(idx_all[:, c], idx_wrap[:, c], 0.0, float(ROWS - 1),
                                        ALU.max, ALU.min).then_inc(idx_step, 1)
                dve.wait_ge(idx_step, count + 3)

            def chunk(m):
                c = m.mod(2)
                parity = m.mod(4) // 2
                half_block = m.quarter()
                dve.wait_ge(gathered[parity][c], (half_block + 1) * (DMA * CHUNK))
                wait(dve, y_out, m, -2 - c)
                first = (half_block * 2 + parity) * SLOTS
                slots = slice(c * CHUNK, (c + 1) * CHUNK)
                nc.vector.tensor_tensor(
                    scaled[parity][:, slots, :], rows[parity][:, slots, :],
                    x_all[:, bass.ds(first + c * CHUNK, CHUNK)].unsqueeze(2).to_broadcast([P, CHUNK, EMB]),
                    ALU.mult).then_inc(chunk_done, 1)
                if c == 1:
                    wait(dve, chunk_done, m, 1)
                    nc.vector.tensor_tensor(
                        scaled[parity][:, OH_SLOTS:OH_SLOTS + FOLD, :], scaled[parity][:, OH_SLOTS:OH_SLOTS + FOLD, :],
                        scaled[parity][:, OH_SLOTS + FOLD:OH_SLOTS + 2 * FOLD, :], ALU.add).then_inc(bag_folded, 1)
                if c == 1 and m.inside(0, UNITS - 5):
                    nc.vector.tensor_copy(
                        idx_now[parity][:, :],
                        idx_all[:, bass.ds(first + 2 * SLOTS, SLOTS)]).then_inc(idx_ready, 1)

            def shift(n, u):
                wait(dve, scores_out[n], u, 1)
                nc.vector.tensor_reduce(row_max[n][:, :], by_key(ps_s[n]), AX.X, ALU.max).then_inc(max_done[n], 1)
                wait(dve, max_done[n], u, 1)
                wait(dve, exp_done[n], u, 0)
                nc.vector.tensor_tensor(by_key(shifted[n]), by_key(ps_s[n]), over_keys(row_max[n]),
                                        ALU.subtract).then_inc(shift_done[n], 1)

            def normalise(n, u):
                wait(dve, exp_done[n], u, 1)
                nc.vector.tensor_reduce(row_sum[n][:, :], by_key(probs[n]), AX.X, ALU.add).then_inc(sum_done[n], 1)
                wait(dve, sum_done[n], u, 1)
                nc.vector.reciprocal(row_inv[n][:, :], row_sum[n][:, :]).then_inc(inv_done[n], 1)
                wait(dve, inv_done[n], u, 1)
                nc.vector.tensor_tensor(by_key(normed[n]), by_key(probs[n]), over_keys(row_inv[n]),
                                        ALU.mult).then_inc(norm_done[n], 1)
                wait(dve, norm_done[n], u, 1)
                if n == 1:
                    wait(dve, at_ready[1], u, 0)
                    nc.vector.transpose(turned[:, :], normed[n][:, :]).then_inc(turned_ready, 1)
                    return
                wait(dve, o_out[n], u, 0)
                for j in range(GROUP):
                    r = slice(j * FIELDS, (j + 1) * FIELDS)
                    to = at_diag[n][r, :].rearrange("p (b j q) -> p b j q", j=GROUP, q=FIELDS)[:, :, j]
                    last = nc.vector.transpose(to, by_key(normed[n])[r])
                last.then_inc(at_ready[n], 1)

            def queries(u):
                wait(dve, q_out[0], u, 1)
                nc.vector.tensor_scalar(qt[0][:, :], ps_q[:, :], bias[:, 0:1], None, ALU.add).then_inc(q_ready[0], 1)

            def weigh(u):
                wait(dve, relu_done[1], u, 1)
                nc.vector.tensor_tensor(
                    by_key(weighted), by_key(z), logit_w[:, :].unsqueeze(1).to_broadcast([P, UNIT, FIELDS]),
                    ALU.mult).then_inc(weighted_done, 1)

            def logit(u):
                wait(dve, weighted_done, u, 1)
                nc.vector.tensor_reduce(logit_part[:, bass.ds(u.number() * UNIT, UNIT)], by_key(weighted), AX.X,
                                        ALU.add).then_inc(logit_done, 1)

            def sigmoid(n, part):
                dve.wait_ge(exp_out, n + 1)
                nc.vector.tensor_scalar(of_part(denom, part), of_part(expd, part), 1.0, None,
                                        ALU.add).then_inc(denom_ready, 1)
                dve.wait_ge(denom_ready, n + 1)
                nc.vector.reciprocal(of_part(answer, part), of_part(denom, part)).then_inc(answer_ready, 1)

            def step(i):
                if i.inside(0, UNITS - 1):
                    shift(0, i)
                if i.inside(-1, UNITS - 3):
                    chunk(i + 2)
                if i.inside(0, UNITS - 1):
                    normalise(0, i)
                if i.is_number(UNITS):
                    shift(1, i + -1)
                    normalise(1, i + -1)
                    weigh(i + -2)
                    logit(i + -2)
                    sigmoid(0, EARLY)
                    return
                if i.inside(2, UNITS + 1):
                    weigh(i + -2)
                if i.inside(1, UNITS):
                    shift(1, i + -1)
                if i.inside(2, UNITS + 1):
                    logit(i + -2)
                if i.inside(1, UNITS):
                    normalise(1, i + -1)
                if i.inside(-1, UNITS - 2):
                    queries(i + 1)

            dve.wait_ge(idx_loaded, DMA)
            wrap_indices(0, 2, 0)
            for b in range(2):
                nc.vector.tensor_copy(idx_now[b][:, :], idx_all[:, b * SLOTS:(b + 1) * SLOTS]).then_inc(idx_ready, 1)
            wrap_indices(2, BLOCKS, 3)
            nc.vector.memset(xy_wide[:, EMB:P], 0.0).then_inc(consts_ready, 1)
            nc.vector.memset(ones[:, :], 1.0).then_inc(consts_ready, 1)
            for b in range(2):
                nc.vector.memset(y1[b][EMB:P, :], 0.0).then_inc(consts_ready, 1)
            nc.vector.memset(w1[EMB:P, :, :], 0.0).then_inc(consts_ready, 1)
            for n in range(2):
                nc.vector.memset(k_diag[n][:, :], 0.0).then_inc(consts_ready, 1)
                nc.vector.memset(at_diag[n][:, :], 0.0).then_inc(consts_ready, 1)
            dve.wait_ge(const_loaded, 5 * DMA)
            nc.vector.tensor_tensor(out_bias[:, :], bias[:, 2::4], bias[:, 3::4], ALU.add).then_inc(consts_ready, 1)
            nc.vector.tensor_tensor(
                ctns_diag[:, :].rearrange("p (s c) -> p s c", c=CONT),
                ctns_t[:, :].unsqueeze(2).to_broadcast([CONT, SAMPLES, CONT]),
                ident[0:CONT, 0:CONT].unsqueeze(1).to_broadcast([CONT, SAMPLES, CONT]),
                ALU.mult).then_inc(consts_ready, 1)
            halves = ident[:, :].rearrange("p (f h s) -> p h f s", f=MULTI, h=2)
            nc.vector.tensor_tensor(bag_sum[:, :].rearrange("p (f s) -> p f s", f=MULTI),
                                    halves[:, 0], halves[:, 1], ALU.add).then_inc(consts_ready, 1)
            nc.vector.tensor_scalar(neg_logit_b[:, :], logit_b[:, :], -1.0, None, ALU.mult).then_inc(consts_ready, 1)
            dve.wait_ge(layer_loaded, 3 * DMA)
            dve.wait_ge(x_loaded, DMA)
            chunk(Unit(None, 0))
            run_units(dve, -1, UNITS + 1, step)

            sigmoid(1, LATE)


def kernel(**inputs):
    import numpy as np
    import concourse.bacc as bacc
    from concourse.bass_utils import run_bass_kernel_spmd

    def get(name):
        return np.asarray(inputs[name if name.startswith("r_") else "L0_rec_" + name])

    def by_slot(onehot, multi):
        oh = onehot.reshape(BLOCKS, BLOCK, QUARTERS, OH_SLOTS).transpose(2, 1, 0, 3)
        mh = multi.reshape(MULTI, BLOCKS, BLOCK, 2, MH_SLOTS).transpose(0, 3, 2, 1, 4)
        mh = mh.reshape(QUARTERS, BLOCK, BLOCKS, MH_SLOTS)
        return np.ascontiguousarray(np.concatenate([oh, mh], axis=3).reshape(P, BLOCKS * SLOTS))

    def layer(n):
        return np.ascontiguousarray(np.stack([get(f"{m}W{n}").T for m in "QKVR"], axis=1))

    arrays = {
        "idx": by_slot(get("r_onehot_i"), get("r_mh_i")),
        "x": by_slot(get("onehot_x"), get("mh_x")),
        "ctns_t": np.ascontiguousarray(get("ctns").T),
        "xx": np.ascontiguousarray(get("xx")),
        "xy": np.ascontiguousarray(get("xy")),
        "ident": np.eye(P, dtype=np.float32),
        "w1": layer(1),
        "w2": layer(2),
        "bias": np.ascontiguousarray(np.stack([get(f"{m}b{n}") for n in (1, 2) for m in "QKVR"], axis=1)),
        "logit_w": np.ascontiguousarray(get("logitW").reshape(FIELDS, HD).T),
        "logit_b": np.ascontiguousarray(np.broadcast_to(get("logitb"), (P, 1))),
    }
    nc = bacc.Bacc("TRN2", target_bir_lowering=False, num_devices=1)
    aps = {k: nc.dram_tensor(f"in_{k}", v.shape, mybir.dt.from_np(v.dtype), kind="ExternalInput").ap()
           for k, v in arrays.items()}
    out = nc.dram_tensor("out_0", (SAMPLES,), F32, kind="ExternalOutput").ap()
    build(nc, aps, out)
    r = run_bass_kernel_spmd(nc, [{f"in_{k}": v for k, v in arrays.items()}], core_ids=[0])
    return r.results[0]["out_0"]
```
